# Optimizing a Trainium2 kernel written in Bass

```python
import numpy as np
import jax
import jax.numpy as jnp

def _softmax(x, axis=-1):
    return jax.nn.softmax(x, axis=axis)

def _gelu(x):
    return jax.nn.gelu(x, approximate=True)

def _silu(x):
    return jax.nn.silu(x)

def _sigmoid(x):
    return jax.nn.sigmoid(x)

def _layernorm(x, axis=-1, eps=1e-05):
    m = jnp.mean(x, axis=axis, keepdims=True)
    v = jnp.var(x, axis=axis, keepdims=True)
    return (x - m) / jnp.sqrt(v + eps)

def _scatter_add(tgt, idx, src, axis=0):
    return tgt.at[idx].add(src)

def _segment_sum(src, seg, n):
    return jax.ops.segment_sum(src, seg, n)
kernel_name = 'mk_rec_standalone_d1_rec_r8_bc6aee'

def setup_inputs(seed: int=0):
    np.random.seed(seed)
    _w = jnp.asarray

    def _rec_inputs():
        import jax
        import jax.numpy as jnp
        _rk = jax.random.key(seed)
        r_x = -0.000392918 + 0.999932 * jax.random.normal(jax.random.fold_in(_rk, 1), (512, 1024), jnp.float32)
        return r_x
    r_x = _rec_inputs()

    def _L0_rec_setup():
        import jax, jax.numpy as jnp
        import numpy as np
        B = 2048
        D = 1024
        E = 8
        T = 2
        H1, H2 = (1024, 512)
        DO = 256
        TH1, TH2 = (512, 256)

        def _glorot(key, shape):
            fan_in, fan_out = (shape[-2], shape[-1])
            s = jnp.sqrt(2.0 / (fan_in + fan_out)).astype(jnp.float32)
            return jax.random.normal(key, shape, dtype=jnp.float32) * s
        key = jax.random.key(seed)
        ks = jax.random.split(key, 16)
        return {'x': jax.random.normal(ks[0], (B, D), dtype=jnp.float32), 'eW1': _glorot(ks[1], (E, D, H1)), 'eb1': jnp.zeros((E, H1), jnp.float32), 'eW2': _glorot(ks[2], (E, H1, H2)), 'eb2': jnp.zeros((E, H2), jnp.float32), 'eW3': _glorot(ks[3], (E, H2, DO)), 'eb3': jnp.zeros((E, DO), jnp.float32), 'gW': _glorot(ks[4], (T, D, E)), 'gb': jnp.zeros((T, E), jnp.float32), 'tW1': _glorot(ks[5], (T, DO, TH1)), 'tb1': jnp.zeros((T, TH1), jnp.float32), 'tW2': _glorot(ks[6], (T, TH1, TH2)), 'tb2': jnp.zeros((T, TH2), jnp.float32), 'tW3': _glorot(ks[7], (T, TH2, 1)), 'tb3': jnp.zeros((T, 1), jnp.float32)}
    _L0_rec_all = _L0_rec_setup()
    _L0_rec_in = {k: v for k, v in _L0_rec_all.items() if k in ('eW1', 'eb1', 'eW2', 'eb2', 'eW3', 'eb3', 'gW', 'gb', 'tW1', 'tb1', 'tW2', 'tb2', 'tW3', 'tb3')}
    del _L0_rec_all
    return {'r_x': r_x, 'L0_rec_eW1': _L0_rec_in['eW1'], 'L0_rec_eb1': _L0_rec_in['eb1'], 'L0_rec_eW2': _L0_rec_in['eW2'], 'L0_rec_eb2': _L0_rec_in['eb2'], 'L0_rec_eW3': _L0_rec_in['eW3'], 'L0_rec_eb3': _L0_rec_in['eb3'], 'L0_rec_gW': _L0_rec_in['gW'], 'L0_rec_gb': _L0_rec_in['gb'], 'L0_rec_tW1': _L0_rec_in['tW1'], 'L0_rec_tb1': _L0_rec_in['tb1'], 'L0_rec_tW2': _L0_rec_in['tW2'], 'L0_rec_tb2': _L0_rec_in['tb2'], 'L0_rec_tW3': _L0_rec_in['tW3'], 'L0_rec_tb3': _L0_rec_in['tb3']}

def reference(r_x, L0_rec_eW1, L0_rec_eb1, L0_rec_eW2, L0_rec_eb2, L0_rec_eW3, L0_rec_eb3, L0_rec_gW, L0_rec_gb, L0_rec_tW1, L0_rec_tb1, L0_rec_tW2, L0_rec_tb2, L0_rec_tW3, L0_rec_tb3):
    import jax
    import jax.numpy as jnp

    def _L0_rec_ref(x, eW1, eb1, eW2, eb2, eW3, eb3, gW, gb, tW1, tb1, tW2, tb2, tW3, tb3):
        import jax, jax.numpy as jnp
        import numpy as np
        B = 2048
        D = 1024
        E = 8
        T = 2
        H1, H2 = (1024, 512)
        DO = 256
        TH1, TH2 = (512, 256)

        def _glorot(key, shape):
            fan_in, fan_out = (shape[-2], shape[-1])
            s = jnp.sqrt(2.0 / (fan_in + fan_out)).astype(jnp.float32)
            return jax.random.normal(key, shape, dtype=jnp.float32) * s
        h = jax.nn.relu(jnp.einsum('bi,eio->beo', x, eW1) + eb1)
        h = jax.nn.relu(jnp.einsum('beh,eho->beo', h, eW2) + eb2)
        expert_out = jnp.einsum('beh,eho->beo', h, eW3) + eb3
        gates = jax.nn.softmax(jnp.einsum('bi,tie->bte', x, gW) + gb, axis=-1)
        tin = jnp.einsum('bte,bed->btd', gates, expert_out)
        th = jax.nn.relu(jnp.einsum('btd,tdh->bth', tin, tW1) + tb1)
        th = jax.nn.relu(jnp.einsum('bth,tho->bto', th, tW2) + tb2)
        out = jax.nn.sigmoid(jnp.einsum('bth,tho->bto', th, tW3) + tb3)
        return out[..., 0]
    y = _L0_rec_ref(r_x, L0_rec_eW1, L0_rec_eb1, L0_rec_eW2, L0_rec_eb2, L0_rec_eW3, L0_rec_eb3, L0_rec_gW, L0_rec_gb, L0_rec_tW1, L0_rec_tb1, L0_rec_tW2, L0_rec_tb2, L0_rec_tW3, L0_rec_tb3)
    return y

_drawn_inputs = setup_inputs


def setup_inputs(seed=0):
    import zlib

    import numpy as np

    out = dict(_drawn_inputs(seed))
    spreads = {'L0_rec_eb1': (0.0, 0.653),
     'L0_rec_eb2': (0.0, 0.493),
     'L0_rec_eb3': (0.0, 0.429),
     'L0_rec_gb': (0.0, 0.541),
     'L0_rec_tb1': (0.0, 0.1),
     'L0_rec_tb2': (0.0, 0.1),
     'L0_rec_tb3': (0.0, 0.28)}
    factors = {}
    for name, (base, spread) in spreads.items():
        noise = np.random.default_rng([zlib.crc32(name.encode()), seed]).standard_normal(out[name].shape)
        drawn = base * np.exp(spread * noise) if base else spread * noise
        out[name] = jnp.asarray(drawn.astype(out[name].dtype))
    for name, factor in factors.items():
        out[name] = (out[name] * factor).astype(out[name].dtype)
    return out
```

```python
from contextlib import ExitStack

import concourse.bass as bass
from concourse import mybir

ALU = mybir.AluOpType
ACT = mybir.ActivationFunctionType
AX = mybir.AxisListType
F32 = mybir.dt.float32
F32R = mybir.dt.float32r

P = 128
DMA = 16

BATCH, D = 512, 1024
E, T = 8, 2
H1, H2, DO = 1024, 512, 256
TH1, TH2 = 512, 256

KX = D // P
K2 = H1 // P
K3 = H2 // P
MG = 4
KT1, KT2 = DO // P, TH1 // P
BT = BATCH // P

PIECE = 2 * MG * P
GROUP_PIECES = KX // 2
PIECES = 3 * GROUP_PIECES
RAW = 6
RING = 4
TILES = H1 // P + H2 // P
TOWER_PIECES = 2 * T
OUT3 = DO // P
GATED = OUT3 * T

BANK_HIDDEN1 = [4, 5, 6, 7, 0, 1, 2, 3]
BANK_HIDDEN2 = [6, 7, 0, 1]
BANK_OUT3 = [4, 5]
BANK_LOGITS, BANK_GATES = 4, 5
BANK_TOWER1 = [[0, 1, 2, 3], [6, 7, 4, 5]]
BANK_TOWER2 = [[0, 1], [2, 3]]
BANK_FINAL = 6

SMALL = {}
_at = 0
for _name, _n in [("b1", E * K2), ("b2", E * K3), ("b3", E * OUT3), ("tb1", T * KT2), ("tb2", T * KT1),
                  ("tw3", T * KT1), ("gw", KX * T * E), ("gb", BT * T * E), ("tb3", BT * T)]:
    SMALL[_name] = (_at, _n)
    _at += _n
NSMALL = _at


def moe_towers(nc, xT, eW1, eW2, eW3, tW1, tW2, small, out):
    with ExitStack() as ctx:
        def sb(name, shape, dt=F32):
            return ctx.enter_context(nc.sbuf_tensor(name, [P] + shape, dt))

        def sem(name):
            return ctx.enter_context(nc.semaphore(name))

        x_hi, x_lo = sb("x_hi", [KX, BATCH], F32R), sb("x_lo", [KX, BATCH], F32R)
        h1_hi, h1_lo = sb("h1_hi", [K2, BATCH], F32R), sb("h1_lo", [K2, BATCH], F32R)
        h2_hi, h2_lo = sb("h2_hi", [K3, BATCH], F32R), sb("h2_lo", [K3, BATCH], F32R)
        w_raw = sb("w_raw", [RAW, PIECE])
        w_hi, w_lo = sb("w_hi", [RING, PIECE], F32R), sb("w_lo", [RING, PIECE], F32R)
        w3_raw = sb("w3_raw", [K3 * DO])
        w3_hi, w3_lo = sb("w3_hi", [K3 * DO], F32R), sb("w3_lo", [K3 * DO], F32R)
        gates_all = sb("gates_all", [T * E, BATCH])
        task_in = sb("task_in", [GATED, BATCH])
        gated = sb("gated", [GATED, BATCH])
        stage = sb("stage", [2, BATCH])
        prm = sb("prm", [NSMALL])
        ident = sb("ident", [P])
        logit = sb("logit", [BT * T, E])
        gate = sb("gate", [BT * T, E])
        red = sb("red", [3, BT * T])
        gatesT = sb("gatesT", [BATCH])
        fin = sb("fin", [4, BT * T])
        banks = [ctx.enter_context(nc.psum_tensor(f"bank{b}", [P, BATCH], F32)) for b in range(8)]
        gates_dram = nc.dram_tensor("gates_dram", [T * E, BATCH], F32, kind="Internal").ap()

        def prm_of(name, i, n=1):
            at = SMALL[name][0]
            return prm[:, bass.ds(at + i, n)] if not isinstance(i, int) else prm[:, at + i:at + i + n]

        x_raw = gates_all[:, 0:KX, :]

        x_landed = [sem(f"x_landed{k}") for k in range(KX)]
        w_landed = [sem(f"w_landed{s}") for s in range(RAW)]
        half_landed = sem("half_landed")
        w3_landed = sem("w3_landed")
        small_landed = sem("small_landed")
        x_hi_ready = sem("x_hi_ready")
        x_ready = sem("x_ready")
        half_hi = sem("half_hi")
        half_ready = sem("half_ready")
        w_hi_ready = sem("w_hi_ready")
        w_ready = sem("w_ready")
        w3_hi_ready = sem("w3_hi_ready")
        w3_ready = sem("w3_ready")
        piece_used = sem("piece_used")
        sums_done = sem("sums_done")
        staged = sem("staged")
        stage_hi = sem("stage_hi")
        hidden_ready = sem("hidden_ready")
        out3_done = sem("out3_done")
        gated_ready = sem("gated_ready")
        added = sem("added")
        zeroed = sem("zeroed")
        ident_ready = sem("ident_ready")
        logits_done = sem("logits_done")
        soft = sem("soft")
        exp_done = sem("exp_done")
        gates_ready = sem("gates_ready")
        gates_turned = sem("gates_turned")
        gates_stored = sem("gates_stored")
        gates_landed = sem("gates_landed")
        tail_gated = sem("tail_gated")
        tin_hi_ready = sem("tin_hi_ready")
        tin_ready = sem("tin_ready")
        tower1_done = sem("tower1_done")
        tower1_staged = sem("tower1_staged")
        tower1_hi = sem("tower1_hi")
        tower1_ready = sem("tower1_ready")
        tower2_done = sem("tower2_done")
        tower2_ready = sem("tower2_ready")
        final_done = sem("final_done")
        fin_step = sem("fin_step")
        fin_exp = sem("fin_exp")
        out_stored = sem("out_stored")

        block = ctx.enter_context(nc.Block())

        w1_dram = eW1.rearrange("e (k p) m -> e p k m", p=P)
        w2_dram = eW2.rearrange("e (k p) m -> e p k m", p=P)
        w3_dram = eW3.rearrange("e (k p) m -> e p k m", p=P)
        x_dram = xT.rearrange("(k p) b -> k p b", p=P)

        def one(e):
            return bass.ds(e, 1) if not isinstance(e, int) else slice(e, e + 1)

        def piece_dram(e, j):
            group, i = divmod(j, GROUP_PIECES)
            if group == 2:
                src = w2_dram[one(e), :, 2 * i:2 * i + 2, :]
            else:
                src = w1_dram[one(e), :, 2 * i:2 * i + 2, group * MG * P:(group + 1) * MG * P]
            return src.rearrange("e p k m -> (e p) k m")

        def raw_piece(j):
            return w_raw[:, j % RAW, :]

        def w3_load_dram(e):
            return w3_dram[one(e)].rearrange("e p k m -> (e p) k m")

        def triple(pe, bank, weights_hi, weights_lo, moving_hi, moving_lo, first, last):
            pe.matmul(bank[:], weights_hi, moving_hi, start=first, stop=False)
            pe.matmul(bank[:], weights_hi, moving_lo, start=False, stop=False)
            return pe.matmul(bank[:], weights_lo, moving_hi, start=False, stop=last)

        @block.sync
        def _(sp):
            def load_piece(e, j, free):
                if free is not None:
                    sp.wait_ge(w_ready, free)
                sp.dma_start(raw_piece(j).rearrange("p (k m) -> p k m", k=2),
                             piece_dram(e, j)).then_inc(w_landed[j % RAW], DMA)

            half = MG * P
            sp.dma_start(x_raw[:, 0, :], x_dram[0]).then_inc(x_landed[0], DMA)
            sp.dma_start(w_raw[:, 0, 0:half], w1_dram[0, :, 0, 0:half]).then_inc(half_landed, DMA)
            sp.dma_start(x_raw[:, 1, :], x_dram[1]).then_inc(x_landed[1], DMA)
            sp.dma_start(w_raw[:, 0, half:], w1_dram[0, :, 1, 0:half]).then_inc(w_landed[0], DMA)
            sp.dma_start(prm[:], small).then_inc(small_landed, DMA)
            for j in range(1, PIECES):
                if j < GROUP_PIECES:
                    for k in (2 * j, 2 * j + 1):
                        sp.dma_start(x_raw[:, k, :], x_dram[k]).then_inc(x_landed[k], DMA)
                load_piece(0, j, j - RAW + 1 if j >= RAW else None)
            sp.dma_start(w3_raw[:].rearrange("p (k m) -> p k m", k=K3), w3_load_dram(0)).then_inc(w3_landed, DMA)
            with sp.Fori(1, E) as e:
                for j in range(PIECES):
                    load_piece(e, j, e * PIECES + (j - RAW + 1))
                    if j == 3:
                        sp.wait_ge(w3_ready, e)
                        sp.dma_start(w3_raw[:].rearrange("p (k m) -> p k m", k=K3),
                                     w3_load_dram(e)).then_inc(w3_landed, DMA)
            for i in range(TOWER_PIECES):
                g = E * PIECES + i
                t = i % T
                src = (tW1 if i < T else tW2)[t].rearrange("(k p) m -> p k m", p=P)
                sp.wait_ge(w_ready, g - RAW + 1)
                sp.dma_start(raw_piece(g).rearrange("p (k m) -> p k m", k=src.shape[1]),
                             src).then_inc(w_landed[g % RAW], DMA)
            sp.wait_ge(fin_step, 4)
            sp.dma_start(out.rearrange("(p b) t -> p (b t)", p=P), fin[:, 3, :]).then_inc(out_stored, DMA)
            sp.wait_ge(out_stored, DMA)

        @block.tensor
        def _(pe):
            def group(e, j0, bank_of, moving_hi, moving_lo, free, tile_ready, between=None):
                for j in range(j0, j0 + GROUP_PIECES):
                    slot = j % RING
                    if not (isinstance(e, int) and e == 0 and j == 0):
                        pe.wait_ge(w_ready, e * PIECES + j + 1)
                    for kk in range(2):
                        k = 2 * (j - j0) + kk
                        if isinstance(e, int) and e == 0 and j == 0:
                            if kk == 0:
                                pe.wait_ge(half_ready, 1)
                            else:
                                pe.wait_ge(w_ready, 1)
                        tile_ready(k)
                        for m in range(MG):
                            if k == 0:
                                free(m)
                            cols = slice((kk * MG + m) * P, (kk * MG + m + 1) * P)
                            mm = triple(pe, banks[bank_of[m]], w_hi[:, slot, cols], w_lo[:, slot, cols],
                                        moving_hi[:, k, :], moving_lo[:, k, :], k == 0, k == KX - 1)
                            if k == KX - 1:
                                mm.then_inc(sums_done, 1)
                    if slot < RING - 1:
                        mm.then_inc(piece_used, 1)
                    if between is not None and j == j0 + 1:
                        between()

            def layer1(e):
                first = isinstance(e, int)

                def x_tile(k):
                    if first:
                        pe.wait_ge(x_ready, k + 1)

                def free_a(m):
                    if not first:
                        if m < 2:
                            pe.wait_ge(gated_ready, (e - 1) * GATED + 1)
                        else:
                            pe.wait_ge(staged, e * TILES + (m - 1 - MG))
                group(e, 0, BANK_HIDDEN1[0:MG], x_hi, x_lo, free_a, x_tile)

                def free_b(m):
                    if not first:
                        pe.wait_ge(staged, e * TILES + min(m + 3 - MG, 0))

                group(e, GROUP_PIECES, BANK_HIDDEN1[MG:], x_hi, x_lo, free_b, lambda k: None)

            def layer2(e, between=None):
                def h1_tile(k):
                    pe.wait_ge(hidden_ready, e * TILES + k + 1)

                def free_c(m):
                    pe.wait_ge(staged, e * TILES + m + 3)

                group(e, 2 * GROUP_PIECES, BANK_HIDDEN2, h1_hi, h1_lo, free_c, h1_tile, between)

            def layer3(done, hidden_counts, staged_count):
                pe.wait_ge(w3_ready, done)
                for k in range(K3):
                    if k < len(hidden_counts):
                        pe.wait_ge(hidden_ready, hidden_counts[k])
                    for o in range(OUT3):
                        if k == 0 and staged_count is not None:
                            pe.wait_ge(staged, staged_count + o)
                        cols = slice(k * DO + o * P, k * DO + (o + 1) * P)
                        mm = triple(pe, banks[BANK_OUT3[o]], w3_hi[:, cols], w3_lo[:, cols],
                                    h2_hi[:, k, :], h2_lo[:, k, :], k == 0, k == K3 - 1)
                        if k == K3 - 1:
                            mm.then_inc(out3_done, 1)

            def gate_logits():
                pe.wait_ge(small_landed, DMA)
                pe.wait_ge(staged, 1)
                gw0 = SMALL["gw"][0]
                for b in range(BT):
                    for k in range(KX):
                        mm = pe.matmul(banks[BANK_LOGITS][:, b * T * E:(b + 1) * T * E],
                                       x_raw[:, k, b * P:(b + 1) * P],
                                       prm[:, gw0 + k * T * E:gw0 + (k + 1) * T * E],
                                       start=(k == 0), stop=(k == KX - 1))
                mm.then_inc(logits_done, 1)

            def turn_gates():
                pe.wait_ge(ident_ready, 1)
                pe.wait_ge(staged, 2)
                pe.wait_ge(gates_ready, 1)
                for b in range(BT):
                    mm = pe.transpose(banks[BANK_GATES][0:T * E, b * P:(b + 1) * P],
                                      gate[:].rearrange("p (b t) e -> p b (t e)", b=BT)[:, b, :], ident[:])
                mm.then_inc(gates_turned, 1)

            layer1(0)
            gate_logits()
            layer2(0, between=turn_gates)
            with pe.Fori(1, E) as e:
                layer1(e)
                layer3(e, [e * TILES], e * TILES + 1)
                layer2(e)
            hid = E * TILES - MG
            pe.wait_ge(gated_ready, (E - 1) * GATED + 1)
            layer3(E, [hid + 1, hid + 2, hid + 3, hid + 4], None)

            g = E * PIECES
            for t in range(T):
                pe.wait_ge(w_ready, g + t + 1)
                slot = (g + t) % RING
                for k in range(KT1):
                    pe.wait_ge(tin_ready, t * OUT3 + k + 1)
                    for m in range(KT2):
                        if k == 0 and BANK_TOWER1[t][m] in BANK_HIDDEN2:
                            pe.wait_ge(staged, E * TILES)
                        if k == 0 and BANK_TOWER1[t][m] in BANK_OUT3:
                            n = (T - 1) * OUT3 + BANK_OUT3.index(BANK_TOWER1[t][m])
                            pe.wait_ge(tail_gated, 2 * n + 1)
                        cols = slice(k * TH1 + m * P, k * TH1 + (m + 1) * P)
                        mm = triple(pe, banks[BANK_TOWER1[t][m]], w_hi[:, slot, cols], w_lo[:, slot, cols],
                                    x_hi[:, t * OUT3 + k, :], x_lo[:, t * OUT3 + k, :], k == 0, k == KT1 - 1)
                        if k == KT1 - 1:
                            mm.then_inc(tower1_done, 1)
            for t in range(T):
                pe.wait_ge(w_ready, g + T + t + 1)
                slot = (g + T + t) % RING
                for k in range(KT2):
                    pe.wait_ge(tower1_ready, t * KT2 + k + 1)
                    for m in range(KT1):
                        if k == 0:
                            pe.wait_ge(tower1_staged, BANK_TOWER2[t][m] + 1)
                        cols = slice(k * TH2 + m * P, k * TH2 + (m + 1) * P)
                        mm = triple(pe, banks[BANK_TOWER2[t][m]], w_hi[:, slot, cols], w_lo[:, slot, cols],
                                    h1_hi[:, t * KT2 + k, :], h1_lo[:, t * KT2 + k, :], k == 0, k == KT2 - 1)
                        if k == KT2 - 1:
                            mm.then_inc(tower2_done, 1)
            for t in range(T):
                for b in range(BT):
                    for k in range(KT1):
                        if b == 0:
                            pe.wait_ge(tower2_ready, t * KT1 + k + 1)
                        mm = pe.matmul(banks[BANK_FINAL][:, b * T + t:b * T + t + 1],
                                       gated[:, t * KT1 + k, :].rearrange("p (q b) -> p q b", b=BT)[:, :, b],
                                       prm_of("tw3", t * KT1 + k), start=(k == 0), stop=(k == KT1 - 1))
            mm.then_inc(final_done, 1)

        @block.scalar
        def _(act):
            def split_hi(e, j):
                act.wait_ge(w_landed[j % RAW], (e * (PIECES // RAW) + j // RAW + 1) * DMA)
                if not isinstance(e, int) or e > 0 or j >= RING:
                    before, slot = e * (PIECES // RING) + (j // RING - 1), j % RING
                    if slot < RING - 1:
                        act.wait_ge(piece_used, before * (RING - 1) + slot + 1)
                    else:
                        act.wait_ge(sums_done, before * MG + MG)
                act.activation(w_hi[:, j % RING, :], raw_piece(j), ACT.Copy).then_inc(w_hi_ready, 1)

            def split3_hi(done):
                act.wait_ge(w3_landed, done * DMA)
                act.wait_ge(gated_ready, (done - 1) * GATED + 1)
                act.activation(w3_hi[:], w3_raw[:], ACT.Copy).then_inc(w3_hi_ready, 1)

            def take_tile(n, i, bias):
                act.wait_ge(sums_done, n + 1)
                if not isinstance(n, int) or n >= 2:
                    act.wait_ge(hidden_ready, n - 1)
                bank = (BANK_HIDDEN1 + BANK_HIDDEN2)[i]
                act.activation(stage[:, i % 2, :], banks[bank][:], ACT.Relu, bias=bias).then_inc(staged, 1)

            def take_hidden1(e, tiles):
                for i in tiles:
                    take_tile(e * TILES + i, i, prm_of("b1", e * K2 + i))

            def take_hidden2(e_next):
                for m in range(MG):
                    take_tile(e_next * TILES - MG + m, K2 + m, prm_of("b2", e_next * K3 - K3 + m))

            def expert(e):
                for j in range(PIECES):
                    if j == GROUP_PIECES - 1 and not isinstance(e, int):
                        take_hidden2(e)
                    if j == 2 * GROUP_PIECES - 1:
                        take_hidden1(e, range(0, MG))
                    if j == 3 * GROUP_PIECES - 1:
                        take_hidden1(e, range(MG, 2 * MG))
                    split_hi(e, j)
                    if j == 1 and not isinstance(e, int):
                        split3_hi(e)

            half = MG * P
            act.wait_ge(half_landed, DMA)
            act.activation(w_hi[:, 0, 0:half], w_raw[:, 0, 0:half], ACT.Copy).then_inc(half_hi, 1)
            act.wait_ge(w_landed[0], DMA)
            act.activation(w_hi[:, 0, half:], w_raw[:, 0, half:], ACT.Copy).then_inc(w_hi_ready, 1)
            for j in range(1, PIECES):
                if j == 2 * GROUP_PIECES - 1:
                    act.wait_ge(small_landed, DMA)
                    take_hidden1(0, range(0, MG))
                if j == 3 * GROUP_PIECES - 1:
                    take_hidden1(0, range(MG, 2 * MG))
                split_hi(0, j)
            act.wait_ge(soft, 3)
            act.activation(gate[:], logit[:], ACT.Exp).then_inc(exp_done, 1)

            with act.Fori(1, E) as e:
                expert(e)

            take_hidden2(E)
            split3_hi(E)
            for i in range(TOWER_PIECES):
                split_hi(E, i)
            for n in range(GATED):
                act.wait_ge(tail_gated, 2 * n + 2)
                act.activation(x_hi[:, n, :], task_in[:, n, :], ACT.Copy).then_inc(tin_hi_ready, 1)
            for n in range(T * KT2):
                t, m = divmod(n, KT2)
                act.wait_ge(tower1_done, n + 1)
                if n >= 2:
                    act.wait_ge(tower1_ready, n - 1)
                act.activation(stage[:, n % 2, :], banks[BANK_TOWER1[t][m]][:], ACT.Relu,
                               bias=prm_of("tb1", n)).then_inc(tower1_staged, 1)
            for n in range(T * KT1):
                t, m = divmod(n, KT1)
                act.wait_ge(tower2_done, n + 1)
                act.activation(gated[:, n, :], banks[BANK_TOWER2[t][m]][:], ACT.Relu,
                               bias=prm_of("tb2", n)).then_inc(tower2_ready, 1)
            act.wait_ge(fin_step, 1)
            act.activation(fin[:, 1, :], fin[:, 0, :], ACT.Exp, scale=-1.0).then_inc(fin_exp, 1)

        @block.vector
        def _(dve):
            def split_lo(g, j):
                dve.wait_ge(w_hi_ready, g + 1)
                dve.tensor_tensor(w_lo[:, j % RING, :], raw_piece(j), w_hi[:, j % RING, :].bitcast(F32),
                                  ALU.subtract).then_inc(w_ready, 1)

            def split3_lo(done):
                dve.wait_ge(w3_hi_ready, done)
                dve.tensor_tensor(w3_lo[:], w3_raw[:], w3_hi[:].bitcast(F32),
                                  ALU.subtract).then_inc(w3_ready, 1)

            def split_tile(n, i, hi, lo):
                dve.wait_ge(staged, n + 1)
                dve.tensor_copy(hi, stage[:, i % 2, :]).then_inc(stage_hi, 1)
                dve.wait_ge(stage_hi, n + 1)
                dve.tensor_tensor(lo, stage[:, i % 2, :], hi.bitcast(F32),
                                  ALU.subtract).then_inc(hidden_ready, 1)

            def split_hidden1(e, tiles):
                for i in tiles:
                    split_tile(e * TILES + i, i, h1_hi[:, i, :], h1_lo[:, i, :])

            def split_hidden2(e_next):
                for m in range(MG):
                    split_tile(e_next * TILES - MG + m, K2 + m, h2_hi[:, m, :], h2_lo[:, m, :])

            def gate_expert(e_next):
                dve.wait_ge(gates_landed, DMA)
                for o in range(OUT3):
                    dve.wait_ge(out3_done, e_next * OUT3 - OUT3 + o + 1)
                    for t in range(T):
                        n = o * T + t
                        if n == 0:
                            dve.wait_ge(added, (e_next - 1) * GATED + 1)
                        at = e_next + (t * E - 1)
                        dve.scalar_tensor_tensor(gated[:, n, :], banks[BANK_OUT3[o]][:],
                                                 prm_of("b3", e_next * OUT3 - OUT3 + o),
                                                 gates_all[:, one(at), :].rearrange("p e b -> p (e b)"),
                                                 ALU.add, ALU.mult).then_inc(gated_ready, 1)

            def expert(e):
                later = not isinstance(e, int)
                for j in range(PIECES):
                    if j == GROUP_PIECES - 1 and later:
                        split_hidden2(e)
                    if j == 2 * GROUP_PIECES - 1:
                        split_hidden1(e, range(0, MG))
                    if j == 3 * GROUP_PIECES - 1:
                        split_hidden1(e, range(MG, 2 * MG))
                    split_lo(e * PIECES + j, j)
                    if j == 1 and later:
                        split3_lo(e)

            def split_x(k):
                dve.wait_ge(x_landed[k], DMA)
                dve.tensor_copy(x_hi[:, k, :], x_raw[:, k, :]).then_inc(x_hi_ready, 1)
                dve.wait_ge(x_hi_ready, k + 1)
                dve.tensor_tensor(x_lo[:, k, :], x_raw[:, k, :], x_hi[:, k, :].bitcast(F32),
                                  ALU.subtract).then_inc(x_ready, 1)

            half = MG * P
            split_x(0)
            dve.wait_ge(half_hi, 1)
            dve.tensor_tensor(w_lo[:, 0, 0:half], w_raw[:, 0, 0:half], w_hi[:, 0, 0:half].bitcast(F32),
                              ALU.subtract).then_inc(half_ready, 1)
            split_x(1)
            dve.wait_ge(w_hi_ready, 1)
            dve.tensor_tensor(w_lo[:, 0, half:], w_raw[:, 0, half:], w_hi[:, 0, half:].bitcast(F32),
                              ALU.subtract).then_inc(w_ready, 1)
            for j in range(1, PIECES):
                if j < GROUP_PIECES:
                    split_x(2 * j)
                    split_x(2 * j + 1)
                if j == 2 * GROUP_PIECES - 1:
                    split_hidden1(0, range(0, MG))
                if j == 3 * GROUP_PIECES - 1:
                    split_hidden1(0, range(MG, 2 * MG))
                split_lo(j, j)

            wide = [P, BT * T, E]
            dve.wait_ge(logits_done, 1)
            dve.wait_ge(small_landed, DMA)
            dve.tensor_tensor(logit[:].rearrange("p n e -> p (n e)"), banks[BANK_LOGITS][:, 0:BT * T * E],
                              prm_of("gb", 0, BT * T * E), ALU.add).then_inc(soft, 1)
            dve.wait_ge(soft, 1)
            dve.tensor_reduce(red[:, 0, :], logit[:], AX.X, ALU.max).then_inc(soft, 1)
            dve.wait_ge(soft, 2)
            dve.tensor_tensor(logit[:], logit[:], red[:, 0, :].unsqueeze(2).broadcast_to(wide),
                              ALU.subtract).then_inc(soft, 1)
            dve.wait_ge(exp_done, 1)
            dve.tensor_reduce(red[:, 1, :], gate[:], AX.X, ALU.add).then_inc(soft, 1)
            dve.wait_ge(soft, 4)
            dve.reciprocal(red[:, 2, :], red[:, 1, :]).then_inc(soft, 1)
            dve.wait_ge(soft, 5)
            dve.tensor_tensor(gate[:], gate[:], red[:, 2, :].unsqueeze(2).broadcast_to(wide),
                              ALU.mult).then_inc(gates_ready, 1)
            dve.wait_ge(gates_turned, 1)
            dve.tensor_copy(gatesT[0:T * E, :], banks[BANK_GATES][0:T * E, :]).then_inc(gated_ready, 1)

            with dve.Fori(1, E) as e:
                expert(e)
                gate_expert(e)

            split_hidden2(E)
            split3_lo(E)
            for i in range(TOWER_PIECES):
                g = E * PIECES + i
                split_lo(g, g)
            dve.wait_ge(added, (E - 1) * GATED + 1)
            step = 0
            for n in range(GATED):
                t, o = divmod(n, OUT3)
                dve.wait_ge(out3_done, (E - 1) * OUT3 + o + 1)
                dve.scalar_tensor_tensor(gated[:, n, :], banks[BANK_OUT3[o]][:], prm_of("b3", (E - 1) * OUT3 + o),
                                         gates_all[:, t * E + E - 1, :], ALU.add, ALU.mult) \
                    .then_inc(tail_gated, 1)
                dve.wait_ge(tail_gated, 2 * n + 1)
                dve.tensor_tensor(task_in[:, n, :], task_in[:, n, :], gated[:, n, :],
                                  ALU.add).then_inc(tail_gated, 1)
                dve.wait_ge(tin_hi_ready, n + 1)
                dve.tensor_tensor(x_lo[:, n, :], task_in[:, n, :], x_hi[:, n, :].bitcast(F32),
                                  ALU.subtract).then_inc(tin_ready, 1)
            for n in range(T * KT2):
                dve.wait_ge(tower1_staged, n + 1)
                dve.tensor_copy(h1_hi[:, n, :], stage[:, n % 2, :]).then_inc(tower1_hi, 1)
                dve.wait_ge(tower1_hi, n + 1)
                dve.tensor_tensor(h1_lo[:, n, :], stage[:, n % 2, :], h1_hi[:, n, :].bitcast(F32),
                                  ALU.subtract).then_inc(tower1_ready, 1)
            dve.wait_ge(final_done, 1)
            dve.tensor_tensor(fin[:, 0, :], banks[BANK_FINAL][:, 0:BT * T], prm_of("tb3", 0, BT * T),
                              ALU.add).then_inc(fin_step, 1)
            dve.wait_ge(fin_exp, 1)
            dve.tensor_scalar(fin[:, 2, :], fin[:, 1, :], 1.0, None, ALU.add).then_inc(fin_step, 2)
            dve.wait_ge(fin_step, 3)
            dve.reciprocal(fin[:, 3, :], fin[:, 2, :]).then_inc(fin_step, 1)

        @block.gpsimd
        def _(pool):
            pool.memset(ident[:], 0.0).then_inc(zeroed, 1)
            pool.memset(task_in[:], 0.0).then_inc(added, 1)
            pool.wait_ge(zeroed, 1)
            pool.affine_select(out=ident[:], in_=ident[:], pattern=[[-1, P]], compare_op=ALU.not_equal,
                               fill=1.0, base=0, channel_multiplier=1).then_inc(ident_ready, 1)
            pool.wait_ge(gated_ready, 1)
            pool.dma_start(gates_dram, gatesT[0:T * E, :]).then_inc(gates_stored, DMA)
            pool.wait_ge(gates_stored, DMA)
            pool.wait_ge(logits_done, 1)
            pool.wait_ge(x_ready, KX)
            pool.dma_start(gates_all[:], gates_dram.partition_broadcast(P)).then_inc(gates_landed, DMA)
            pool.wait_ge(added, 1)
            with pool.Fori(1, E) as e:
                for o in range(OUT3):
                    for t in range(T):
                        n = o * T + t
                        pool.wait_ge(gated_ready, e * GATED - GATED + n + 2)
                        pool.tensor_tensor(task_in[:, t * OUT3 + o, :], task_in[:, t * OUT3 + o, :],
                                           gated[:, n, :], ALU.add).then_inc(added, 1)


def kernel(r_x, L0_rec_eW1, L0_rec_eb1, L0_rec_eW2, L0_rec_eb2, L0_rec_eW3, L0_rec_eb3, L0_rec_gW, L0_rec_gb,
           L0_rec_tW1, L0_rec_tb1, L0_rec_tW2, L0_rec_tb2, L0_rec_tW3, L0_rec_tb3):
    import numpy as np
    import concourse.bacc as bacc
    from concourse.bass_utils import run_bass_kernel_spmd

    def per_partition(a, n):
        a = np.asarray(a)
        return a.reshape(-1, n, P).transpose(2, 0, 1).reshape(P, -1)

    small = np.concatenate([
        per_partition(L0_rec_eb1, K2), per_partition(L0_rec_eb2, K3), per_partition(L0_rec_eb3, OUT3),
        per_partition(L0_rec_tb1, KT2), per_partition(L0_rec_tb2, KT1),
        per_partition(np.asarray(L0_rec_tW3).reshape(T, TH2), KT1),
        np.asarray(L0_rec_gW).reshape(T, KX, P, E).transpose(2, 1, 0, 3).reshape(P, -1),
        np.broadcast_to(np.asarray(L0_rec_gb).reshape(1, 1, T * E), (P, BT, T * E)).reshape(P, -1),
        np.broadcast_to(np.asarray(L0_rec_tb3).reshape(1, 1, T), (P, BT, T)).reshape(P, -1),
    ], axis=1)
    arrays = {
        "xT": np.ascontiguousarray(np.asarray(r_x).T),
        "eW1": np.asarray(L0_rec_eW1), "eW2": np.asarray(L0_rec_eW2), "eW3": np.asarray(L0_rec_eW3),
        "tW1": np.asarray(L0_rec_tW1), "tW2": np.asarray(L0_rec_tW2),
        "small": np.ascontiguousarray(small),
    }
    nc = bacc.Bacc("TRN2", target_bir_lowering=False, num_devices=1)
    aps = [nc.dram_tensor(n, a.shape, F32, kind="ExternalInput").ap() for n, a in arrays.items()]
    aps.append(nc.dram_tensor("out", (BATCH, T), F32, kind="ExternalOutput").ap())
    moe_towers(nc, *aps)
    r = run_bass_kernel_spmd(nc, [arrays], core_ids=[0])
    return r.results[0]["out"]
```
